# Optimizing a Trainium2 kernel written in Bass

```python
import numpy as np
import jax
import jax.numpy as jnp

def _softmax(x, axis=-1):
    return jax.nn.softmax(x, axis=axis)
def _gelu(x):
    return jax.nn.gelu(x, approximate=True)
def _silu(x):
    return jax.nn.silu(x)
def _sigmoid(x):
    return jax.nn.sigmoid(x)
def _layernorm(x, axis=-1, eps=1e-5):
    m = jnp.mean(x, axis=axis, keepdims=True)
    v = jnp.var(x, axis=axis, keepdims=True)
    return (x - m) / jnp.sqrt(v + eps)
def _scatter_add(tgt, idx, src, axis=0):
    return tgt.at[idx].add(src)
def _segment_sum(src, seg, n):
    return jax.ops.segment_sum(src, seg, n)

kernel_name = 'mk_adj_ffn_d1_adj_512_662e4a'

def setup_inputs(seed: int = 0):
    np.random.seed(seed)
    _w = jnp.asarray
    def _rec_inputs():
        import jax
        import jax.numpy as jnp
        _gk = jax.random.key(seed)
        x = -0.0002928 + 1 * jax.random.normal(jax.random.fold_in(_gk, 1), (2708, 512), jnp.float32)
        _a = jax.random.bernoulli(jax.random.fold_in(_gk, 2), 0.00295421, (2708, 2708))
        _a = jnp.logical_or(_a, jnp.eye(2708, dtype=bool))
        _af = _a.astype(jnp.float32)
        adj = _af
        return x, adj
    x, adj = _rec_inputs()
    def _L0_gnn_setup():
        import jax, jax.numpy as jnp
        import numpy as np
        N = 8192
        F_IN = 512
        F_OUT = 512
        DENSITY = 0.01
        key = jax.random.key(seed)
        k_x, k_adj, k_w, k_b = jax.random.split(key, 4)
        input_features = jax.random.normal(k_x, (N, F_IN), dtype=jnp.float32)
        adj = (jax.random.uniform(k_adj, (N, N)) < DENSITY).astype(jnp.float32)
        idx = jnp.arange(N)
        adj = adj.at[idx, idx].set(1.0)
        W = jax.random.normal(k_w, (F_IN, F_OUT), dtype=jnp.float32) / np.sqrt(F_IN)
        b = jax.random.normal(k_b, (F_OUT,), dtype=jnp.float32) * 0.01
        return {'input_features': input_features, 'adj': adj, 'W': W, 'b': b}
    _L0_gnn_all = _L0_gnn_setup()
    _L0_gnn_in = {k: v for k, v in _L0_gnn_all.items() if k in ('W', 'b', )}
    del _L0_gnn_all

    def _L0_ffn_setup():
        import jax, jax.numpy as jnp
        import numpy as np
        B, S, D, E, H, TOP_K = (16, 4096, 512, 8, 1024, 2)
        key = jax.random.key(seed)
        ks = jax.random.split(key, 6)
        x = jax.random.normal(ks[0], (B, S, D), jnp.float32)
        gate_w = jax.random.normal(ks[1], (D, E), jnp.float32) * 0.02
        gate_b = jnp.zeros((E,), jnp.float32)
        w1 = jax.random.normal(ks[2], (E, D, H), jnp.float32) * 0.02
        b1 = jnp.zeros((E, H), jnp.float32)
        w2 = jax.random.normal(ks[3], (E, H, D), jnp.float32) * 0.02
        b2 = jnp.zeros((E, D), jnp.float32)
        return {'x': x, 'gate_w': gate_w, 'gate_b': gate_b, 'w1': w1, 'b1': b1, 'w2': w2, 'b2': b2}
    _L0_ffn_all = _L0_ffn_setup()
    _L0_ffn_in = {k: v for k, v in _L0_ffn_all.items() if k in ('gate_w', 'gate_b', 'w1', 'b1', 'w2', 'b2', )}
    del _L0_ffn_all

    return {
        "x": x,
        "adj": adj,
        "L0_gnn_W": _L0_gnn_in["W"],
        "L0_gnn_b": _L0_gnn_in["b"],
        "L0_ffn_gate_w": _L0_ffn_in["gate_w"],
        "L0_ffn_gate_b": _L0_ffn_in["gate_b"],
        "L0_ffn_w1": _L0_ffn_in["w1"],
        "L0_ffn_b1": _L0_ffn_in["b1"],
        "L0_ffn_w2": _L0_ffn_in["w2"],
        "L0_ffn_b2": _L0_ffn_in["b2"],
    }

def reference(x, adj, L0_gnn_W, L0_gnn_b, L0_ffn_gate_w, L0_ffn_gate_b, L0_ffn_w1, L0_ffn_b1, L0_ffn_w2, L0_ffn_b2):
    import jax
    import jax.numpy as jnp
    def _L0_gnn_ref(input_features, adj, W, b):
        import jax, jax.numpy as jnp
        import numpy as np
        N = 8192
        F_IN = 512
        F_OUT = 512
        DENSITY = 0.01
        A = (adj != 0).astype(input_features.dtype)
        hidden = input_features @ W + b
        deg = jnp.sum(A, axis=0)
        return A @ hidden / deg[:, None]

    def _L0_ffn_ref(x, gate_w, gate_b, w1, b1, w2, b2):
        import jax, jax.numpy as jnp
        import numpy as np
        B, S, D, E, H, TOP_K = (16, 4096, 512, 8, 1024, 2)
        orig_shape = x.shape
        xf = x.reshape(-1, orig_shape[-1])
        T = xf.shape[0]
        n_experts = gate_w.shape[-1]
        scores = jax.nn.softmax(xf @ gate_w + gate_b, axis=-1)
        top_w, top_i = jax.lax.top_k(scores, TOP_K)
        top_w = top_w / top_w.sum(axis=-1, keepdims=True)
        combine = jnp.zeros((T, n_experts), xf.dtype).at[jnp.arange(T)[:, None], top_i].add(top_w)
        out = jnp.zeros_like(xf)
        for e in range(n_experts):
            h = jax.nn.gelu(xf @ w1[e] + b1[e], approximate=False)
            out = out + combine[:, e:e + 1] * (h @ w2[e] + b2[e])
        return out.reshape(orig_shape)

    x = x + _L0_gnn_ref(_layernorm(x, axis=-1), adj, L0_gnn_W, L0_gnn_b)
    x = x + _L0_ffn_ref((_layernorm(x, axis=-1))[None], L0_ffn_gate_w, L0_ffn_gate_b, L0_ffn_w1, L0_ffn_b1, L0_ffn_w2, L0_ffn_b2)[0]
    return x


_drawn_inputs = setup_inputs


def setup_inputs(seed=0):
    import zlib

    import numpy as np

    out = dict(_drawn_inputs(seed))
    spreads = {'L0_ffn_gate_b': (0.0, 0.1), 'L0_ffn_b1': (0.0, 0.325), 'L0_ffn_b2': (0.0, 0.1)}
    factors = {'L0_gnn_b': 3.552}
    for name, (base, spread) in spreads.items():
        noise = np.random.default_rng([zlib.crc32(name.encode()), seed]).standard_normal(out[name].shape)
        drawn = base * np.exp(spread * noise) if base else spread * noise
        out[name] = jnp.asarray(drawn.astype(out[name].dtype))
    for name, factor in factors.items():
        out[name] = (out[name] * factor).astype(out[name].dtype)
    return out
```

```python
from contextlib import ExitStack

import concourse.bass as bass
from concourse import mybir

F32 = mybir.dt.float32
F16 = mybir.dt.float16
I32 = mybir.dt.int32
U32 = mybir.dt.uint32
U16 = mybir.dt.uint16
ALU = mybir.AluOpType
ACT = mybir.ActivationFunctionType
AX_X = mybir.AxisListType.X

P = 128
EPS = 1e-5
WSCALE = 256.0
UNSCALE = 1.0 / WSCALE


class Chain:

    def __init__(self, engine, sem, per_item, apart=None):
        self.engine, self.sem, self.per_item, self.apart = engine, sem, per_item, apart

    def start(self, item):
        self.base, self.k = item * self.per_item, 0

    def __call__(self, instruction):
        self.k += 1
        instruction.then_inc(self.sem, 1)
        self.engine.wait_ge(self.sem, self.base + self.k)
        if self.apart is not None:
            self.engine.sem_inc(self.apart, 1)

    def end(self):
        assert self.k == self.per_item, (self.k, self.per_item)


def build(nc, x, adj, W, b, gate_w, gate_b, w1, b1, w2, b2, out):
    N, D = x.shape
    E, _, H = w1.shape
    NT = (N + P - 1) // P
    LAST = NT - 1
    LAST_ROWS = N - LAST * P
    KD, KH = D // P, H // P
    HALF_BLOCKS = NT // 2
    HALF = HALF_BLOCKS * P
    HALF_COLS = [HALF, N - HALF]
    assert NT % 2 == 0 and D == 512 and H == 1024 and E == 8
    REGION = (NT + 1) * P
    TILES = (2 * N + E * (P - 1)) // P
    TILES += TILES % 2
    REC = 2 * D + 8
    CH = 1024
    NCH = 2 * KD
    WSET = NCH * 2 * CH

    records = nc.dram_tensor("records", (E * REGION + P, REC), U16).ap()

    def rows(i):
        return LAST_ROWS if isinstance(i, int) and i == LAST else P

    with ExitStack() as ctx:
        def place(name, shape, dtype, at):
            return nc.alloc_sbuf_tensor_at(name, shape, dtype, offset=at)

        size = {F32: 4, F16: 2, I32: 4, U32: 4}

        class Region:
            def __init__(self, start, end):
                self.at, self.limit = start, end

            def take(self, name, shape, dtype):
                n = size[dtype]
                for d in shape[1:]:
                    n *= d
                t = place(name, shape, dtype, self.at)
                self.at += (n + 31) // 32 * 32
                assert self.at <= self.limit, (name, self.at, self.limit)
                return t

        base = (nc.sbuf_base + 31) // 32 * 32
        top = nc.sbuf_usable_end // 32 * 32
        main = Region(base, top)
        AT0 = main.at
        AT = main.take("AT", [P, LAST, NT, P], F16)
        AT_END = main.at
        ATL = main.take("ATL", [P, NT, 32], F16)
        HID0 = main.at
        HID = main.take("HID", [P, NT, 2, D], F16)

        ident = main.take("ident", [P, P], F16)
        tri = main.take("tri", [P, P], F16)
        ones = main.take("ones", [P, P], F16)
        ident32 = main.take("ident32", [64, 64], F32)
        b1T = main.take("b1T", [P, E * KH], F32)
        gw16 = main.take("gw16", [P, KD, 2, E], F16)
        gb = main.take("gb", [P, E], F32)
        iota8 = main.take("iota8", [P, E], F32)
        region_base = main.take("region_base", [P, E], F32)
        region_row = main.take("region_row", [P, E], F32)
        thr = main.take("thr", [P, NT - 1], F32)
        tile_no = main.take("tile_no", [P, TILES], F32)
        token = main.take("token", [P, 1], F32)
        mhalf = main.take("mhalf", [P, 1], F32)
        padmask = main.take("padmask", [P, NT], F32)
        rdeg = main.take("rdeg", [P, NT], F32)
        msum = main.take("msum", [P, E], F16)
        etab = main.take("etab", [P, TILES], F32)
        wall = main.take("wall", [P, TILES], F32)
        idxall = main.take("idxall", [P, TILES], U32)
        tab_row = main.take("tab_row", [1, TILES], I32)
        tab_expert = main.take("tab_expert", [1, TILES], I32)
        tab_woff = main.take("tab_woff", [1, TILES], I32)
        tab_end = main.take("tab_end", [1, E], I32)
        bn = main.take("bn", [P, 2, 6], F32)
        mv = main.take("mv", [P, 2, 2], F32)
        ve = main.take("ve", [P, 2], F32)
        rstd = main.take("rstd", [P, 2], F32)
        scratch = main.at

        s1 = Region(scratch, top)
        A32 = [s1.take(f"A32_{h}", [P, HALF], F32) for h in range(2)]
        A16 = [s1.take(f"A16_{h}", [P, HALF], F16) for h in range(2)]
        x32 = [s1.take(f"x32_{s}", [P, D], F32) for s in range(2)]
        xs = [s1.take(f"xs_{s}", [P, 2 * D], F16) for s in range(2)]
        xT = [s1.take(f"xT_{s}", [P, 2 * KD, P], F16) for s in range(2)]
        W16 = s1.take("W16", [P, 2, KD, D], F16)
        bbc = s1.take("bbc", [P, D], F32)
        hid32 = s1.take("hid32", [P, D], F32)
        st = Region(HID0 + 12 * 2048, HID0 + 20 * 2048)
        Wst = st.take("Wst", [P, KD, D], F32)
        gwst = st.take("gwst", [P, KD, E], F32)
        b1st = st.take("b1st", [64, P], F32)

        s2 = Region(scratch, top)
        xr = [s2.take(f"xr_{s}", [P, D], F32) for s in range(2)]
        x1 = [s2.take(f"x1_{s}", [P, D], F32) for s in range(2)]
        rec = [s2.take(f"rec_{s}", [P, REC], F16) for s in range(2)]
        xT2 = s2.take("xT2", [P, 2 * KD, P], F16)
        stage = [s2.take(f"stage_{s}", [P, CH], F32) for s in range(2)]
        padrec = s2.take("padrec", [P, REC], F16)
        lg = s2.take("lg", [P, 2, E], F32)
        ex = s2.take("ex", [P, E], F32)
        pr = s2.take("pr", [P, E], F32)
        top_l = s2.take("top_l", [P, E], F32)
        top_p = s2.take("top_p", [P, E], F32)
        top_i = s2.take("top_i", [P, E], U32)
        sm = s2.take("sm", [P, 16], F32)
        oh = s2.take("oh", [P, 2, E], F32)
        m16 = [s2.take(f"m16_{s}", [P, E], F16) for s in range(2)]
        place_e = s2.take("place_e", [P, E], F32)
        junk = s2.take("junk", [P, 2, E], F32)
        slotf = s2.take("slotf", [P, 2], F32)
        slots = [s2.take(f"slots_{s}", [P, 2], U32) for s in range(2)]
        padidx = s2.take("padidx", [P, E], U32)
        cnt = s2.take("cnt", [P, E], F32)
        cmp = s2.take("cmp", [P, E, NT - 1], F32)
        ntile = s2.take("ntile", [P, E], F32)
        cum = [s2.take(f"cum_{k}", [P, E], F32) for k in range(4)]
        ge = s2.take("ge", [P, E, TILES], F32)
        gt = s2.take("gt", [P, E, TILES], F32)
        tb = s2.take("tb", [P, 6, TILES], F32)
        tbi = s2.take("tbi", [1, 2, TILES], I32)

        s3 = Region(AT0, AT_END)
        WS = s3.take("WS", [P, 2 * WSET], F16)
        b2bc = s3.take("b2bc", [P, E * D], F32)
        B2_TILES = (s3.at - AT0 + NT * P * 2 - 1) // (NT * P * 2)
        r3 = [s3.take(f"r3_{s}", [P, REC], F16) for s in range(2)]
        xT3 = [s3.take(f"xT3_{s}", [P, 2 * KD, P], F16) for s in range(2)]
        h32 = [s3.take(f"h32_{s}", [P, H], F32) for s in range(2)]
        h16 = [s3.take(f"h16_{s}", [P, 2, H], F16) for s in range(2)]
        ybuf = s3.take("ybuf", [P, 4, D], F32)
        yout = s3.take("yout", [P, D], F32)
        yidx = s3.take("yidx", [P, 1], U32)

        psT = ctx.enter_context(nc.psum_tensor("psT", [P, 2 * KD, P], F16))
        psA = ctx.enter_context(nc.psum_tensor("psA", [P, 2, D], F32))
        psB = ctx.enter_context(nc.psum_tensor("psB", [P, 4, 512], F32))
        psC = ctx.enter_context(nc.psum_tensor("psC", [P, 512], F32))
        psAT = [psB[:, 2 * h:2 * h + 2, :].bitcast(F16).rearrange("p a b -> p (a b)") for h in range(2)]
        psL, psR = psB[:, 0, 0:E], psB[:, 1, 0:E]

        def sem(name):
            return ctx.enter_context(nc.semaphore(name))

        consts = sem("consts")
        pool_waited = sem("pool_waited")
        dve_waited = sem("dve_waited")
        pool_setup = sem("pool_setup")
        w_loaded = sem("w_loaded")
        small_loaded = sem("small_loaded")
        w_high = sem("w_high")
        w_split = sem("w_split")
        b1_turned = sem("b1_turned")
        b1_ready = sem("b1_ready")
        x_loaded = [sem(f"x_loaded_{s}") for s in range(2)]
        A_loaded = [sem(f"A_loaded_{h}") for h in range(2)]
        stats_step = sem("stats_step")
        stats_done = sem("stats_done")
        rstd_step = sem("rstd_step")
        rstd_done = sem("rstd_done")
        xn_done = sem("xn_done")
        xhigh_done = sem("xhigh_done")
        xs_ready = sem("xs_ready")
        xs_turned = sem("xs_turned")
        xT_ready = sem("xT_ready")
        A_binary = sem("A_binary")
        A_turned = sem("A_turned")
        A_stored = sem("A_stored")
        hid_done = sem("hid_done")
        hid32_done = sem("hid32_done")
        hidhigh_done = sem("hidhigh_done")
        hid_ready = sem("hid_ready")
        deg_step = sem("deg_step")
        xr_loaded = [sem(f"xr_loaded_{s}") for s in range(2)]
        x1_stored = [sem(f"x1_stored_{s}") for s in range(2)]
        acc_done = sem("acc_done")
        x1_done = sem("x1_done")
        stats2_done = sem("stats2_done")
        rstd2_step = sem("rstd2_step")
        rstd2_done = sem("rstd2_done")
        xn2_done = sem("xn2_done")
        rechigh_done = sem("rechigh_done")
        rec_ready = sem("rec_ready")
        rec_turned = sem("rec_turned")
        xT2_ready = sem("xT2_ready")
        logits_done = sem("logits_done")
        neg_max_ready = sem("neg_max_ready")
        exp_done = sem("exp_done")
        route_step = sem("route_step")
        m_ready = sem("m_ready")
        rank_done = sem("rank_done")
        slot_step = sem("slot_step")
        slot_ready = sem("slot_ready")
        scattered = [sem(f"scattered_{s}") for s in range(2)]
        pad_step = sem("pad_step")
        pad_ready = sem("pad_ready")
        pads_written = sem("pads_written")
        spare_written = sem("spare_written")
        counts_done = sem("counts_done")
        table_step = sem("table_step")
        padidx_ready = sem("padidx_ready")
        tables_ready = sem("tables_ready")
        chunk_loaded = [sem(f"chunk_loaded_{s}") for s in range(2)]
        prep_step = sem("prep_step")
        weights_ready = sem("weights_ready")
        b2_loaded = sem("b2_loaded")
        r3_loaded = [sem(f"r3_loaded_{s}") for s in range(2)]
        r3_turned = sem("r3_turned")
        xT3_step = sem("xT3_step")
        xT3_ready = sem("xT3_ready")
        up_done = sem("up_done")
        gelu_done = sem("gelu_done")
        hhigh_done = sem("hhigh_done")
        h_ready = sem("h_ready")
        down_done = sem("down_done")
        y_read = sem("y_read")
        y_ready = sem("y_ready")
        y_copied = sem("y_copied")
        added = sem("added")

        block = ctx.enter_context(nc.Block())

        def row_tile(ap, i):
            return ap[i * P:i * P + rows(i)] if isinstance(i, int) else ap[bass.ds(i * P, P)]

        def over_tiles(engine, step, tail):
            for n in range(4):
                step(n, n % 2)
            with engine.Fori(2, NT // 2 - 1) as pair:
                step(2 * pair, 0)
                step(2 * pair + 1, 1)
            for n in range(NT - 2, NT + tail):
                step(n, n % 2)

        def live(i):
            return not isinstance(i, int) or 0 <= i < NT

        def later(i, k=1):
            return not isinstance(i, int) or i >= k

        @block.sync
        def _(sp):
            sp.dma_start(Wst[:, :, :], W.rearrange("(k p) f -> p k f", p=P)).then_inc(w_loaded, 16)

            def load_1(n, s):
                if not live(n):
                    return
                if later(n, 2):
                    sp.wait_ge(xs_ready, n - 1)
                sp.dma_start(x32[s][0:rows(n), :], row_tile(x, n)).then_inc(x_loaded[s], 16)
                if isinstance(n, int) and n == 0:
                    sp.dma_start(bbc[:, :], b.partition_broadcast(P)).then_inc(small_loaded, 16)
                    sp.dma_start(gb[:, :], gate_b.partition_broadcast(P)).then_inc(small_loaded, 16)
                    sp.dma_start(gwst[:, :, :], gate_w.rearrange("(k p) e -> p k e", p=P)).then_inc(small_loaded, 16)
                    sp.dma_start(b1st[:, :], b1.rearrange("e (c p) -> (e c) p", p=P)).then_inc(small_loaded, 16)
                for h in range(2):
                    if later(n):
                        sp.wait_ge(A_binary, 2 * n + h - 1)
                    sp.dma_start(A32[h][0:rows(n), 0:HALF_COLS[h]],
                                 row_tile(adj, n)[:, h * HALF:h * HALF + HALF_COLS[h]]).then_inc(A_loaded[h], 16)

            over_tiles(sp, load_1, 0)

            sp.wait_ge(hid_ready, NT)
            sp.wait_ge(A_stored, 2 * NT)
            sp.wait_ge(pad_ready, 1)
            sp.dma_start(out[N:N + P], padrec[:, 0:2 * D].bitcast(F32)).then_inc(spare_written, 16)
            sp.dma_start(records[E * REGION:E * REGION + P], padrec[:, :].bitcast(U16)).then_inc(spare_written, 16)
            sp.dma_start(xr[0][:, :], row_tile(x, 0)).then_inc(xr_loaded[0], 16)

            def move_2(n, s):
                if not live(n):
                    return
                if not isinstance(n, int) or n + 1 < NT:
                    if later(n):
                        sp.wait_ge(rec_ready, n)
                    sp.dma_start(xr[1 - s][0:rows(n + 1), :], row_tile(x, n + 1)).then_inc(xr_loaded[1 - s], 16)
                sp.wait_ge(x1_done, n + 1)
                sp.dma_start(row_tile(out, n), x1[s][0:rows(n), :]).then_inc(x1_stored[s], 16)

            over_tiles(sp, move_2, 0)
            sp.wait_ge(acc_done, NT)
            sp.dma_start(b2bc[:, :], b2.rearrange("e d -> (e d)").partition_broadcast(P)).then_inc(b2_loaded, 16)

            for s in range(2):
                sp.wait_ge(scattered[s], 16 * NT)
            sp.wait_ge(pads_written, 16 * E)
            sp.wait_ge(spare_written, 32)
            sp.wait_ge(tables_ready, 1)

            def load_3(g, s, turn):
                row = sp.value_load(tab_row[0:1, bass.ds(g, 1)], min_val=0, max_val=E * REGION)
                if later(g, 2):
                    sp.wait_ge(xT3_ready, g - 1)
                sp.dma_start(r3[s][:, :].bitcast(U16), records[bass.ds(row, P)]).then_inc(r3_loaded[s], 16)

            load_3(0, 0, 0)
            load_3(1, 1, 0)
            with sp.Fori(1, TILES // 2) as pair:
                load_3(2 * pair, 0, pair)
                load_3(2 * pair + 1, 1, pair)

        @block.gpsimd
        def _(pool):
            setup_step = [0]

            def setup(instruction):
                setup_step[0] += 1
                instruction.then_inc(pool_setup, 1)
                pool.wait_ge(pool_setup, setup_step[0])

            nc.gpsimd.memset(A16[1][:, HALF_COLS[1]:HALF], 0.0)
            nc.gpsimd.memset(ones[:, :], 1.0)
            nc.gpsimd.memset(mhalf[:, :], -0.5)
            setup(nc.gpsimd.memset(ident[:, :], 0.0))
            setup(nc.gpsimd.affine_select(out=ident[:, :], in_=ident[:, :], compare_op=ALU.not_equal, fill=1.0,
                                          base=0, pattern=[[1, P]], channel_multiplier=-1))
            nc.gpsimd.memset(ident32[:, :], 0.0).then_inc(pool_setup, 1)
            setup_step[0] += 1
            setup(nc.gpsimd.affine_select(out=tri[:, :], in_=ones[:, :], compare_op=ALU.is_gt, fill=0.0,
                                          base=0, pattern=[[1, P]], channel_multiplier=-1))
            nc.gpsimd.affine_select(out=ident32[:, :], in_=ident32[:, :], compare_op=ALU.not_equal, fill=1.0,
                                    base=0, pattern=[[1, 64]], channel_multiplier=-1)
            nc.gpsimd.memset(HID[:, LAST, :, :], 0.0)
            nc.gpsimd.memset(msum[:, :], 0.0)
            setup(nc.gpsimd.memset(padmask[:, :], 0.0))
            nc.gpsimd.affine_select(out=padmask[:, :], in_=padmask[:, :], compare_op=ALU.is_gt, fill=1.0,
                                    base=N, pattern=[[-P, NT]], channel_multiplier=-1)
            for t, pattern, start, mult in (
                (iota8, [[1, E]], 0, 0),
                (region_base, [[REGION, E]], 0, 0),
                (region_row, [[REGION, E]], 0, 1),
                (thr, [[P, NT - 1]], P, 0),
                (tile_no, [[1, TILES]], 0, 0),
            ):
                nc.gpsimd.iota(t[:, :], pattern, base=start, channel_multiplier=mult,
                               allow_small_or_imprecise_dtypes=True)
            nc.gpsimd.iota(token[:, :], [[0, 1]], base=0, channel_multiplier=1,
                           allow_small_or_imprecise_dtypes=True).then_inc(consts, 1)

            pow_step = Chain(pool, rstd_step, 1, pool_waited)
            pow2_step = Chain(pool, rstd2_step, 1, pool_waited)

            def reciprocal_std(i, s, chain, stats, done):
                r = rows(i)
                pool.wait_ge(stats, i + 1)
                pool.sem_inc(pool_waited, 1)
                chain.start(i)
                chain(nc.gpsimd.tensor_scalar(ve[0:r, s:s + 1], mv[0:r, s, 1:2], EPS, None, ALU.add))
                nc.gpsimd.tensor_tensor(rstd[0:r, s:s + 1], ve[0:r, s:s + 1], mhalf[0:r, :], ALU.pow).then_inc(done, 1)

            def norm_1(n, s):
                if live(n):
                    reciprocal_std(n, s, pow_step, stats_done, rstd_done)
                    r = rows(n)
                    pool.wait_ge(xhigh_done, n + 1)
                    nc.gpsimd.tensor_tensor(xs[s][0:r, D:2 * D], x32[s][0:r, :], xs[s][0:r, 0:D],
                                            ALU.subtract).then_inc(xs_ready, 1)
                if live(n - 2):
                    i, r = n - 2, rows(n - 2)
                    pool.wait_ge(hidhigh_done, i + 1)
                    nc.gpsimd.tensor_tensor(HID[0:r, i, 1, :], hid32[0:r, :], HID[0:r, i, 0, :],
                                            ALU.subtract).then_inc(hid_ready, 1)

            over_tiles(pool, norm_1, 2)

            pool.wait_ge(A_stored, 2 * NT)
            nc.gpsimd.memset(padrec[:, :], 0.0).then_inc(pad_step, 1)
            pool.wait_ge(pad_step, 1)
            nc.gpsimd.iota(padrec[:, 2 * D:2 * D + 2].bitcast(U32), [[0, 1]], base=N, channel_multiplier=1)
            nc.gpsimd.memset(padrec[:, 2 * D + 6:REC].bitcast(F32), -1.0).then_inc(pad_ready, 1)

            prep = Chain(pool, prep_step, 3, pool_waited)

            def load_chunk(e, q):
                c = q % KD
                if q < KD:
                    src = w1[e, c * P:(c + 1) * P, :]
                    dst = stage[q % 2][:, :]
                else:
                    src = w2[e, 2 * c * P:2 * (c + 1) * P, :].rearrange("(a p) d -> p a d", p=P)
                    dst = stage[q % 2][:, :].rearrange("p (a d) -> p a d", a=2)
                pool.dma_start(dst, src).then_inc(chunk_loaded[q % 2], 16)

            def split_chunk(e, q, wset):
                t, at = stage[q % 2], wset * WSET + q * 2 * CH
                pool.wait_ge(chunk_loaded[q % 2], 16 * (e * (NCH // 2) + q // 2 + 1))
                pool.sem_inc(pool_waited, 1)
                prep.start(e * NCH + q)
                prep(nc.gpsimd.tensor_scalar(t[:, :], t[:, :], WSCALE, None, ALU.mult))
                prep(nc.gpsimd.tensor_copy(WS[:, at:at + CH], t[:, :]))
                last = nc.gpsimd.tensor_tensor(WS[:, at + CH:at + 2 * CH], t[:, :], WS[:, at:at + CH], ALU.subtract)
                prep(last)

            def step_2(n, s):
                if live(n - 2):
                    i, r = n - 2, rows(n - 2)
                    pool.wait_ge(slot_ready, i + 1)
                    pool.sem_inc(pool_waited, 1)
                    for k in range(2):
                        nc.gpsimd.indirect_dma_start(
                            records[:, :], bass.IndirectOffsetOnAxis(ap=slots[s][0:r, k:k + 1], axis=0),
                            rec[s][0:r, :].bitcast(U16), None).then_inc(scattered[s], 16 if k == 0 else 16)
                if live(n):
                    reciprocal_std(n, s, pow2_step, stats2_done, rstd2_done)
                    r = rows(n)
                    pool.wait_ge(rechigh_done, n + 1)
                    nc.gpsimd.tensor_tensor(rec[s][0:r, D:2 * D], xr[s][0:r, :], rec[s][0:r, 0:D],
                                            ALU.subtract).then_inc(rec_ready, 1)

            over_tiles(pool, step_2, 2)

            pool.wait_ge(padidx_ready, 1)
            for e in range(E):
                nc.gpsimd.indirect_dma_start(records[:, :], bass.IndirectOffsetOnAxis(ap=padidx[:, e:e + 1], axis=0),
                                             padrec[:, :].bitcast(U16), None).then_inc(pads_written, 16)

            def prepare_expert(e, wset):
                load_chunk(e, 0)
                for q in range(NCH):
                    if q + 1 < NCH:
                        load_chunk(e, q + 1)
                    split_chunk(e, q, wset)
                nc.gpsimd.engine_nop().then_inc(weights_ready, 1)

            def add_rows(first, end):
                with pool.Fori(first, end) as g:
                    pool.wait_ge(y_ready, g + 1)
                    pool.wait_ge(added, 16 * g)
                    pool.sem_inc(pool_waited, 1)
                    nc.gpsimd.tensor_copy(yout[:, :], ybuf[:, g % 4, :])
                    nc.gpsimd.tensor_copy(yidx[:, :], idxall[:, bass.ds(g, 1)]).then_inc(y_copied, 1)
                    pool.wait_ge(y_copied, g + 1)
                    pool.sem_inc(pool_waited, 1)
                    nc.gpsimd.indirect_dma_start(out[:, :], bass.IndirectOffsetOnAxis(ap=yidx[:, :], axis=0),
                                                 yout[:, :], None, compute_op=ALU.add).then_inc(added, 16)

            pool.wait_ge(acc_done, NT)
            prepare_expert(0, 0)
            prepare_expert(1, 1)
            pool.wait_ge(tables_ready, 1)
            for s in range(2):
                pool.wait_ge(x1_stored[s], 16 * (NT // 2))
            pool.wait_ge(spare_written, 32)

            def tiles_end(e):
                return pool.value_load(tab_end[0:1, e:e + 1] if isinstance(e, int) else tab_end[0:1, bass.ds(e, 1)],
                                       min_val=1, max_val=TILES)

            add_rows(0, tiles_end(0))

            def expert(e, wset):
                first = tiles_end(e - 1)
                pool.wait_ge(down_done, first)
                pool.sem_inc(pool_waited, 1)
                prepare_expert(e + 1, 1 - wset)
                add_rows(tiles_end(e - 1), tiles_end(e))

            with pool.Fori(0, (E - 2) // 2) as pair:
                expert(2 * pair + 1, 1)
                expert(2 * pair + 2, 0)
            add_rows(tiles_end(E - 2), TILES)
            pool.wait_ge(added, 16 * TILES)

        @block.scalar
        def _(act):
            act.wait_ge(w_loaded, 16)
            nc.scalar.activation(W16[:, 0, :, :], Wst[:, :, :], ACT.Copy, scale=WSCALE).then_inc(w_high, 1)
            act.wait_ge(small_loaded, 64)
            nc.scalar.activation(gw16[:, :, 0, :], gwst[:, :, :], ACT.Copy, scale=WSCALE).then_inc(w_high, 1)

            def store_A(n, h):
                act.wait_ge(A_turned, 2 * n + h + 1)
                if isinstance(n, int) and n == LAST:
                    blocks = psAT[h][:, 0:HALF].rearrange("p (j i) -> p j i", i=P)
                    nc.scalar.copy(ATL[:, h * HALF_BLOCKS:(h + 1) * HALF_BLOCKS, 0:LAST_ROWS],
                                   blocks[:, :, 0:LAST_ROWS]).then_inc(A_stored, 1)
                else:
                    nc.scalar.copy(AT[:, n, h * HALF_BLOCKS:(h + 1) * HALF_BLOCKS, :].rearrange("p j i -> p (j i)"),
                                   psAT[h][:, 0:HALF]).then_inc(A_stored, 1)

            def step_1(n, s):
                if live(n):
                    r = rows(n)
                    store_A(n, 0)
                    act.wait_ge(xn_done, n + 1)
                    if later(n, 2):
                        act.wait_ge(xs_turned, n - 1)
                    nc.scalar.copy(xs[s][0:r, 0:D], x32[s][0:r, :]).then_inc(xhigh_done, 1)
                    store_A(n, 1)
                if live(n - 2):
                    i, r = n - 2, rows(n - 2)
                    act.wait_ge(hid32_done, i + 1)
                    nc.scalar.copy(HID[0:r, i, 0, :], hid32[0:r, :]).then_inc(hidhigh_done, 1)

            over_tiles(act, step_1, 2)

            def step_2(n, s):
                if live(n - 2):
                    i, r = n - 2, rows(n - 2)
                    act.wait_ge(neg_max_ready, i + 1)
                    nc.scalar.activation(ex[0:r, :], lg[0:r, 0, :], ACT.Exp, bias=sm[0:r, 0:1],
                                         accum_out=sm[0:r, 1:2]).then_inc(exp_done, 1)
                if live(n):
                    r = rows(n)
                    act.wait_ge(xn2_done, n + 1)
                    if later(n, 2):
                        act.wait_ge(scattered[s], 16 * (n - s))
                    nc.scalar.copy(rec[s][0:r, 0:D], xr[s][0:r, :]).then_inc(rechigh_done, 1)

            over_tiles(act, step_2, 2)

            act.wait_ge(tables_ready, 1)
            act.wait_ge(b1_ready, 1)

            def gelu(g, s):
                e = act.value_load(tab_expert[0:1, bass.ds(g, 1)], min_val=0, max_val=E - 1)
                for half in range(2):
                    act.wait_ge(up_done, 2 * g + half + 1)
                    if half == 0 and later(g, 2):
                        act.wait_ge(h_ready, 2 * g - 2)
                    for c in range(half * 4, half * 4 + 4):
                        last = nc.scalar.activation(
                            h32[s][:, c * P:(c + 1) * P], psB[:, half, (c % 4) * P:(c % 4 + 1) * P], ACT.Gelu,
                            bias=b1T[:, bass.ds(e * KH + c, 1)], scale=UNSCALE)
                    last.then_inc(gelu_done, 1)

            gelu(0, 0)
            gelu(1, 1)
            with act.Fori(1, TILES // 2) as pair:
                gelu(2 * pair, 0)
                gelu(2 * pair + 1, 1)

        @block.vector
        def _(dve):
            dve.wait_ge(w_high, 1)
            nc.vector.scalar_tensor_tensor(W16[:, 1, :, :], Wst[:, :, :], WSCALE, W16[:, 0, :, :],
                                           ALU.mult, ALU.subtract).then_inc(w_split, 1)
            dve.wait_ge(w_high, 2)
            nc.vector.scalar_tensor_tensor(gw16[:, :, 1, :], gwst[:, :, :], WSCALE, gw16[:, :, 0, :],
                                           ALU.mult, ALU.subtract).then_inc(w_split, 1)
            dve.wait_ge(b1_turned, 1)
            nc.vector.tensor_copy(b1T[:, :], psC[:, 0:E * KH]).then_inc(b1_ready, 1)

            stats = Chain(dve, stats_step, 1, dve_waited)

            def statistics(item, i, s, t, done):
                r = rows(i)
                stats.start(item)
                stats(nc.vector.bn_stats(bn[0:r, s, :], t[0:r, :]))
                nc.vector.bn_aggr(mv[0:r, s, :], bn[0:r, s, :]).then_inc(done, 1)

            def binary(n, h):
                r = rows(n)
                dve.wait_ge(A_loaded[h], 16 * (n + 1))
                if later(n):
                    dve.wait_ge(A_turned, 2 * n + h - 1)
                nc.vector.tensor_scalar(A16[h][0:r, 0:HALF_COLS[h]], A32[h][0:r, 0:HALF_COLS[h]], 0.0, None,
                                        ALU.not_equal).then_inc(A_binary, 1)

            def step_1(n, s):
                if live(n):
                    r = rows(n)
                    dve.wait_ge(x_loaded[s], 8 * n + (16 if s == 0 else 8))
                    statistics(n, n, s, x32[s], stats_done)
                    if isinstance(n, int) and n == 0:
                        dve.wait_ge(consts, 1)
                    binary(n, 0)
                    dve.wait_ge(rstd_done, n + 1)
                    nc.vector.tensor_scalar(x32[s][0:r, :], x32[s][0:r, :], mv[0:r, s, 0:1], rstd[0:r, s:s + 1],
                                            ALU.subtract, ALU.mult).then_inc(xn_done, 1)
                    binary(n, 1)
                if live(n - 1):
                    i = n - 1
                    dve.wait_ge(xs_turned, i + 1)
                    if later(i, 2):
                        dve.wait_ge(hid_done, i - 1)
                    nc.vector.tensor_copy(xT[1 - s][:, :, 0:rows(i)], psT[:, :, 0:rows(i)]).then_inc(xT_ready, 1)
                if live(n - 2):
                    i, r = n - 2, rows(n - 2)
                    dve.wait_ge(hid_done, i + 1)
                    if isinstance(i, int) and i == 0:
                        dve.wait_ge(small_loaded, 64)
                    if later(i):
                        dve.wait_ge(hid_ready, i)
                    nc.vector.scalar_tensor_tensor(hid32[0:r, :], psA[0:r, s, :], UNSCALE, bbc[0:r, :],
                                                   ALU.mult, ALU.add).then_inc(hid32_done, 1)

            over_tiles(dve, step_1, 2)

            dve.wait_ge(A_turned, 2 * NT)
            nc.vector.tensor_tensor(rdeg[:, :], psC[:, 0:NT], padmask[:, :], ALU.add).then_inc(deg_step, 1)
            dve.wait_ge(deg_step, 1)
            nc.vector.reciprocal(rdeg[:, :], rdeg[:, :]).then_inc(deg_step, 1)
            dve.wait_ge(deg_step, 2)

            route = Chain(dve, route_step, 14, dve_waited)
            slot = Chain(dve, slot_step, 3)

            def route_tile(i, s):
                r = rows(i)
                route.start(i)
                if isinstance(i, int) and i == LAST:
                    nc.vector.memset(m16[s][:, :], 0.0)
                dve.wait_ge(logits_done, i + 1)
                route(nc.vector.scalar_tensor_tensor(lg[0:r, 0, :], psL[0:r, :], UNSCALE, gb[0:r, :],
                                                     ALU.mult, ALU.add))
                route(nc.vector.max(top_l[0:r, :], lg[0:r, 0, :]))
                nc.vector.tensor_scalar(sm[0:r, 0:1], top_l[0:r, 0:1], -1.0, None, ALU.mult).then_inc(neg_max_ready, 1)
                dve.wait_ge(exp_done, i + 1)
                route(nc.vector.reciprocal(sm[0:r, 2:3], sm[0:r, 1:2]))
                route(nc.vector.tensor_scalar(pr[0:r, :], ex[0:r, :], sm[0:r, 2:3], None, ALU.mult))
                route(nc.vector.max(top_p[0:r, :], pr[0:r, :]))
                route(nc.vector.max_index(top_i[0:r, :], top_p[0:r, :], pr[0:r, :]))
                route(nc.vector.tensor_copy(sm[0:r, 4:6], top_i[0:r, 0:2]))
                route(nc.vector.tensor_tensor(sm[0:r, 6:7], top_p[0:r, 0:1], top_p[0:r, 1:2], ALU.add))
                route(nc.vector.reciprocal(sm[0:r, 7:8], sm[0:r, 6:7]))
                route(nc.vector.tensor_scalar(sm[0:r, 8:10], top_p[0:r, 0:2], sm[0:r, 7:8], None, ALU.mult))
                words = rec[s][:, 2 * D:REC].bitcast(F32)
                nc.vector.tensor_copy(rec[s][0:r, 2 * D:2 * D + 2].bitcast(U32), token[0:r, :])
                nc.vector.tensor_copy(words[0:r, 1:2], sm[0:r, 9:10])
                nc.vector.tensor_tensor(words[0:r, 2:3], sm[0:r, 8:9], sm[0:r, 9:10], ALU.subtract)
                route(nc.vector.tensor_copy(words[0:r, 3:4], sm[0:r, 4:5]))
                route(nc.vector.tensor_scalar(token[:, :], token[:, :], float(P), None, ALU.add))
                route(nc.vector.tensor_scalar(oh[0:r, 0, :], iota8[0:r, :], sm[0:r, 4:5], None, ALU.is_equal))
                route(nc.vector.tensor_scalar(oh[0:r, 1, :], iota8[0:r, :], sm[0:r, 5:6], None, ALU.is_equal))
                nc.vector.tensor_tensor(m16[s][0:r, :], oh[0:r, 0, :], oh[0:r, 1, :], ALU.add).then_inc(m_ready, 1)
                route.end()

            def slot_tile(i, s):
                r = rows(i)
                slot.start(i)
                dve.wait_ge(rank_done, i + 1)
                slot(nc.vector.tensor_tensor(place_e[0:r, :], psR[0:r, :], region_base[0:r, :], ALU.add))
                for k in range(2):
                    slot(nc.vector.tensor_tensor_reduce(junk[0:r, k, :], place_e[0:r, :], oh[0:r, k, :], 1.0, 0.0,
                                                        ALU.mult, ALU.add, slotf[0:r, k:k + 1]))
                nc.vector.tensor_tensor(msum[:, :], msum[:, :], m16[s][:, :], ALU.add)
                nc.vector.tensor_copy(slots[s][0:r, :], slotf[0:r, :]).then_inc(slot_ready, 1)
                slot.end()

            def step_2(n, s):
                if live(n - 2):
                    route_tile(n - 2, s)
                if live(n - 1):
                    i = n - 1
                    dve.wait_ge(rec_turned, i + 1)
                    if later(i):
                        dve.wait_ge(logits_done, i)
                    nc.vector.tensor_copy(xT2[:, :, 0:rows(i)], psT[:, :, 0:rows(i)]).then_inc(xT2_ready, 1)
                if live(n - 2):
                    slot_tile(n - 2, s)
                if live(n):
                    r = rows(n)
                    dve.wait_ge(acc_done, n + 1)
                    dve.wait_ge(xr_loaded[s], 8 * n + (16 if s == 0 else 8))
                    if later(n, 2):
                        dve.wait_ge(x1_stored[s], 8 * n + (0 if s == 0 else -8))
                    nc.vector.scalar_tensor_tensor(x1[s][0:r, :], psA[0:r, s, :],
                                                   rdeg[0:r, n:n + 1] if isinstance(n, int) else rdeg[0:r, bass.ds(n, 1)],
                                                   xr[s][0:r, :], ALU.mult, ALU.add).then_inc(x1_done, 1)
                    dve.wait_ge(x1_done, n + 1)
                    statistics(n + NT, n, s, x1[s], stats2_done)
                    dve.wait_ge(rstd2_done, n + 1)
                    nc.vector.tensor_scalar(xr[s][0:r, :], x1[s][0:r, :], mv[0:r, s, 0:1], rstd[0:r, s:s + 1],
                                            ALU.subtract, ALU.mult).then_inc(xn2_done, 1)

            over_tiles(dve, step_2, 2)

            table_count = [0]

            def table(instruction):
                table_count[0] += 1
                instruction.then_inc(table_step, 1)
                dve.wait_ge(table_step, table_count[0])

            dve.wait_ge(counts_done, 1)
            table(nc.vector.tensor_copy(cnt[:, :], psC[:, 0:E]))
            nc.vector.tensor_tensor(padidx[:, :], cnt[:, :], region_row[:, :], ALU.add).then_inc(padidx_ready, 1)
            table(nc.vector.tensor_tensor(cmp[:, :, :], cnt[:, :].unsqueeze(2).to_broadcast([P, E, NT - 1]),
                                          thr[:, :].unsqueeze(1).to_broadcast([P, E, NT - 1]), ALU.is_gt))
            table(nc.vector.tensor_reduce(ntile[:, :], cmp[:, :, :], AX_X, ALU.add))
            table(nc.vector.tensor_scalar(cum[0][:, :], ntile[:, :], 1.0, None, ALU.add))
            for k, d in enumerate((1, 2, 4)):
                nc.vector.tensor_copy(cum[k + 1][:, 0:d], cum[k][:, 0:d])
                table(nc.vector.tensor_tensor(cum[k + 1][:, d:E], cum[k][:, d:E], cum[k][:, 0:E - d], ALU.add))
            end = cum[3]
            nc.vector.tensor_copy(tab_end[:, :], end[0:1, :])
            table(nc.vector.tensor_tensor(ge[:, :, :], tile_no[:, :].unsqueeze(1).to_broadcast([P, E, TILES]),
                                          end[:, :].unsqueeze(2).to_broadcast([P, E, TILES]), ALU.is_ge))
            table(nc.vector.tensor_tensor(gt[:, :, :], ge[:, :, :], cum[0][:, :].unsqueeze(2).to_broadcast([P, E, TILES]),
                                          ALU.mult))
            table(nc.vector.tensor_reduce(tb[:, 0, :], ge[:, :, :].rearrange("p e g -> p g e"), AX_X, ALU.add))
            table(nc.vector.tensor_scalar(etab[:, :], tb[:, 0, :], float(E - 1), None, ALU.min))
            table(nc.vector.tensor_reduce(tb[:, 1, :], gt[:, 0:E - 1, :].rearrange("p e g -> p g e"), AX_X, ALU.add))
            table(nc.vector.tensor_tensor(tb[:, 2, :], tile_no[:, :], tb[:, 1, :], ALU.subtract))
            table(nc.vector.tensor_scalar(tb[:, 2, :], tb[:, 2, :], float(P), None, ALU.mult))
            table(nc.vector.scalar_tensor_tensor(tb[:, 3, :], etab[:, :], float(REGION), tb[:, 2, :], ALU.mult, ALU.add))
            table(nc.vector.tensor_scalar(tb[:, 4, :], tb[:, 3, :], -1.0, float(E * REGION), ALU.mult, ALU.add))
            table(nc.vector.tensor_tensor(tb[:, 5, :], tb[:, 4, :], ge[:, E - 1, :], ALU.mult))
            table(nc.vector.tensor_tensor(tb[:, 2, :], tb[:, 3, :], tb[:, 5, :], ALU.add))
            nc.vector.tensor_copy(tab_row[:, :], tb[0:1, 2, :])
            table(nc.vector.tensor_copy(tab_expert[:, :], etab[0:1, :]))
            table(nc.vector.tensor_scalar(tbi[:, 0, :], tab_expert[:, :], 1, None, ALU.bitwise_and))
            nc.vector.tensor_scalar(tab_woff[:, :], tbi[:, 0, :], WSET, None, ALU.mult).then_inc(tables_ready, 1)
            dve.wait_ge(tables_ready, 1)

            dve.wait_ge(b2_loaded, 16)
            x_step = Chain(dve, xT3_step, 1)
            half_step = Chain(dve, hhigh_done, 1)

            def take_rows(g, s):
                dve.wait_ge(r3_turned, g + 1)
                col = slice(g, g + 1) if isinstance(g, int) else bass.ds(g, 1)
                words = r3[s][:, 2 * D:REC].bitcast(F32)
                x_step.start(g)
                nc.vector.tensor_copy(idxall[:, col], r3[s][:, 2 * D:2 * D + 2].bitcast(U32))
                x_step(nc.vector.scalar_tensor_tensor(wall[:, col], words[:, 3:4], etab[:, col], words[:, 2:3],
                                                      ALU.is_equal, ALU.mult))
                nc.vector.tensor_tensor(wall[:, col], wall[:, col], words[:, 1:2], ALU.add)
                if later(g, 2):
                    dve.wait_ge(up_done, 2 * g - 2)
                nc.vector.tensor_copy(xT3[s][:, :, :], psT[:, :, :]).then_inc(xT3_ready, 1)

            def split_half(g, s, half):
                cols = slice(half * 512, half * 512 + 512)
                dve.wait_ge(gelu_done, 2 * g + half + 1)
                if half == 0 and later(g, 2):
                    dve.wait_ge(down_done, g - 1)
                half_step.start(2 * g + half)
                half_step(nc.vector.tensor_copy(h16[s][:, 0, cols], h32[s][:, cols]))
                nc.vector.tensor_tensor(h16[s][:, 1, cols], h32[s][:, cols], h16[s][:, 0, cols],
                                        ALU.subtract).then_inc(h_ready, 1)

            def weigh(g, s):
                col = slice(g, g + 1) if isinstance(g, int) else bass.ds(g, 1)
                e = dve.value_load(tab_expert[0:1, col], min_val=0, max_val=E - 1)
                dve.wait_ge(down_done, g + 1)
                if later(g, 4):
                    dve.wait_ge(y_copied, g - 3)
                y = ybuf[:, g % 4, :]
                nc.vector.scalar_tensor_tensor(y, psA[:, s, :], UNSCALE, b2bc[:, bass.ds(e * D, D)],
                                               ALU.mult, ALU.add).then_inc(y_read, 1)
                dve.wait_ge(y_read, g + 1)
                nc.vector.tensor_scalar(y, y, wall[:, col], None, ALU.mult).then_inc(y_ready, 1)

            def step_3(g, s, more=True):
                split_half(g, s, 0)
                if more:
                    take_rows(g + 1, 1 - s)
                split_half(g, s, 1)
                if later(g):
                    weigh(g - 1, 1 - s)

            take_rows(0, 0)
            for g in range(4):
                step_3(g, g % 2)
            with dve.Fori(2, TILES // 2 - 1) as pair:
                step_3(2 * pair, 0)
                step_3(2 * pair + 1, 1)
            step_3(TILES - 2, 0)
            step_3(TILES - 1, 1, more=False)
            weigh(TILES - 1, 1)

        @block.tensor
        def _(pe):
            pe.wait_ge(consts, 1)
            pe.wait_ge(small_loaded, 64)
            nc.tensor.transpose(psC[:, 0:E * KH], b1st[:, :], ident32[:, :]).then_inc(b1_turned, 1)
            pe.wait_ge(b1_ready, 1)

            def turn_A(n, h):
                r = rows(n)
                pe.wait_ge(A_binary, 2 * n + h + 1)
                if later(n):
                    pe.wait_ge(A_stored, 2 * n + h - 1)
                for j in range(HALF_BLOCKS):
                    blk = A16[h][0:r, j * P:(j + 1) * P]
                    nc.tensor.transpose(psAT[h][:, j * P:j * P + r], blk, ident[0:r, 0:r])
                for j in range(HALF_BLOCKS):
                    blk = A16[h][0:r, j * P:(j + 1) * P]
                    c = h * HALF_BLOCKS + j
                    last = nc.tensor.matmul(psC[:, c:c + 1], blk, ones[0:r, 0:1],
                                            start=(isinstance(n, int) and n == 0 and c == 0), stop=False,
                                            skip_group_check=True)
                last.then_inc(A_turned, 1)

            def turn(i, t, ready, taken, done):
                r = rows(i)
                pe.wait_ge(ready, i + 1)
                if later(i):
                    pe.wait_ge(taken, i)
                for k in range(2 * KD):
                    last = nc.tensor.transpose(psT[:, k, 0:r], t[0:r, k * P:(k + 1) * P], ident[0:r, 0:r])
                last.then_inc(done, 1)

            def hidden(i, s):
                r = rows(i)
                pe.wait_ge(xT_ready, i + 1)
                if later(i, 2):
                    pe.wait_ge(hid32_done, i - 1)
                m = 0
                for k in range(KD):
                    for xp, wp in ((0, 0), (0, 1), (1, 0)):
                        last = nc.tensor.matmul(psA[0:r, s, :], xT[s][:, xp * KD + k, 0:r], W16[:, wp, k, :],
                                                start=(m == 0), stop=(m == 3 * KD - 1))
                        m += 1
                last.then_inc(hid_done, 1)

            def step_1(n, s):
                if live(n):
                    turn_A(n, 0)
                if live(n - 1):
                    turn(n - 1, xs[1 - s], xs_ready, xT_ready, xs_turned)
                if live(n):
                    turn_A(n, 1)
                if live(n - 2):
                    if isinstance(n, int) and n == 2:
                        pe.wait_ge(w_split, 2)
                    hidden(n - 2, s)

            over_tiles(pe, step_1, 2)

            pe.wait_ge(hid_ready, NT)
            pe.wait_ge(A_stored, 2 * NT)

            def gather(n, s, first):
                r = rows(n)
                if first:
                    pe.wait_ge(x1_done if later(n, 2) else hid_ready, n - 1 if later(n, 2) else NT)
                for j in range(0 if first else NT // 2, NT // 2 if first else NT):
                    blk = ATL[:, j, 0:r] if isinstance(n, int) and n == LAST else AT[:, n, j, :]
                    for part in range(2):
                        last = nc.tensor.matmul(psA[0:r, s, :], blk, HID[:, j, part, :],
                                                start=(j == 0 and part == 0), stop=(j == NT - 1 and part == 1))
                if not first:
                    last.then_inc(acc_done, 1)

            def router(i, s):
                r = rows(i)
                pe.wait_ge(xT2_ready, i + 1)
                if later(i):
                    pe.wait_ge(neg_max_ready, i)
                m = 0
                for k in range(KD):
                    for xp, wp in ((0, 0), (0, 1), (1, 0)):
                        last = nc.tensor.matmul(psL[0:r, :], xT2[:, xp * KD + k, 0:r], gw16[:, k, wp, :],
                                                start=(m == 0), stop=(m == 3 * KD - 1))
                        m += 1
                last.then_inc(logits_done, 1)

            def rank(i, s):
                pe.wait_ge(m_ready, i + 1)
                if later(i):
                    pe.wait_ge(slot_ready, i)
                nc.tensor.matmul(psR, tri[:, :], m16[s][:, :], start=True, stop=False)
                nc.tensor.matmul(psR, ones[:, :], msum[:, :], start=False, stop=True).then_inc(rank_done, 1)

            def step_2(n, s):
                if live(n):
                    gather(n, s, True)
                if live(n - 1):
                    turn(n - 1, rec[1 - s], rec_ready, xT2_ready, rec_turned)
                if live(n - 2):
                    rank(n - 2, s)
                if live(n):
                    gather(n, s, False)
                if live(n - 1):
                    router(n - 1, 1 - s)

            over_tiles(pe, step_2, 2)

            pe.wait_ge(slot_ready, NT)
            nc.tensor.matmul(psC[:, 0:E], ones[:, :], msum[:, :], start=True, stop=True).then_inc(counts_done, 1)

            pe.wait_ge(tables_ready, 1)

            def turn_rows(g, s):
                pe.wait_ge(r3_loaded[s], 8 * g + (16 if s == 0 else 8))
                if later(g):
                    pe.wait_ge(xT3_ready, g)
                for k in range(2 * KD):
                    last = nc.tensor.transpose(psT[:, k, :], r3[s][:, k * P:(k + 1) * P], ident[:, :])
                last.then_inc(r3_turned, 1)

            def weight_offset(g):
                return pe.value_load(tab_woff[0:1, g:g + 1] if isinstance(g, int) else tab_woff[0:1, bass.ds(g, 1)],
                                     min_val=0, max_val=WSET)

            def up(g, s):
                off = weight_offset(g)
                e = pe.value_load(tab_expert[0:1, g:g + 1] if isinstance(g, int) else tab_expert[0:1, bass.ds(g, 1)],
                                  min_val=0, max_val=E - 1)
                pe.wait_ge(weights_ready, e + 1)
                pe.wait_ge(xT3_ready, g + 1)
                for c in range(KH):
                    half = c // 4
                    if c % 4 == 0 and later(g):
                        pe.wait_ge(gelu_done, 2 * g - 1 + half)
                    m = 0
                    for k in range(KD):
                        for wp, xp in ((0, 0), (0, 1), (1, 0)):
                            last = nc.tensor.matmul(
                                psB[:, half, (c % 4) * P:(c % 4 + 1) * P],
                                WS[:, bass.ds(off + (k * 2 + wp) * CH + c * P, P)], xT3[s][:, xp * KD + k, :],
                                start=(m == 0), stop=(m == 3 * KD - 1))
                            m += 1
                    if c % 4 == 3:
                        last.then_inc(up_done, 1)

            def down(g, s):
                off = weight_offset(g)
                if later(g, 2):
                    pe.wait_ge(y_read, g - 1)
                m = 0
                for c in range(KH):
                    if c % 4 == 0:
                        pe.wait_ge(h_ready, 2 * g + c // 4 + 1)
                    at = ((KD + c // 2) * 2) * CH + (c % 2) * D
                    for hp, wp in ((0, 0), (0, 1), (1, 0)):
                        last = nc.tensor.matmul(psA[:, s, :], h16[s][:, hp, c * P:(c + 1) * P],
                                                WS[:, bass.ds(off + at + wp * CH, D)],
                                                start=(m == 0), stop=(m == 3 * KH - 1))
                        m += 1
                last.then_inc(down_done, 1)

            def step_3(g, s, more=True):
                up(g, s)
                if more:
                    turn_rows(g + 1, 1 - s)
                if later(g):
                    down(g - 1, 1 - s)

            turn_rows(0, 0)
            step_3(0, 0)
            step_3(1, 1)
            with pe.Fori(1, TILES // 2 - 1) as pair:
                step_3(2 * pair, 0)
                step_3(2 * pair + 1, 1)
            step_3(TILES - 2, 0)
            step_3(TILES - 1, 1, more=False)
            down(TILES - 1, 1)


_INS = ["x", "adj", "L0_gnn_W", "L0_gnn_b", "L0_ffn_gate_w", "L0_ffn_gate_b", "L0_ffn_w1", "L0_ffn_b1",
        "L0_ffn_w2", "L0_ffn_b2"]


def kernel(**inputs):
    import numpy as _np
    import concourse.bacc as _bacc
    from concourse import mybir as _mybir
    from concourse.bass_utils import run_bass_kernel_spmd as _run

    nc = _bacc.Bacc("TRN2", target_bir_lowering=False, num_devices=1)
    arrays, args = {}, []
    for name in _INS:
        a = _np.ascontiguousarray(inputs[name])
        arrays[f"in_{name}"] = a
        args.append(nc.dram_tensor(f"in_{name}", a.shape, _mybir.dt.from_np(a.dtype), kind="ExternalInput").ap())
    n, d = arrays["in_x"].shape
    out = nc.dram_tensor("out", (n + 128, d), _mybir.dt.float32, kind="ExternalOutput").ap()
    build(nc, *args, out)
    r = _run(nc, [arrays], core_ids=[0])
    return r.results[0]["out"][:n]
```
